# Optimizing a Trainium2 kernel written in Bass

```python
import numpy as np
import jax
import jax.numpy as jnp

def _softmax(x, axis=-1):
    return jax.nn.softmax(x, axis=axis)

def _gelu(x):
    return jax.nn.gelu(x, approximate=True)

def _silu(x):
    return jax.nn.silu(x)

def _sigmoid(x):
    return jax.nn.sigmoid(x)

def _layernorm(x, axis=-1, eps=1e-05):
    m = jnp.mean(x, axis=axis, keepdims=True)
    v = jnp.var(x, axis=axis, keepdims=True)
    return (x - m) / jnp.sqrt(v + eps)

def _scatter_add(tgt, idx, src, axis=0):
    return tgt.at[idx].add(src)

def _segment_sum(src, seg, n):
    return jax.ops.segment_sum(src, seg, n)
kernel_name = 'mk_adj_ffn_d2_adj_r2_5bfdd3'

def setup_inputs(seed: int=0):
    np.random.seed(seed)
    _w = jnp.asarray

    def _rec_inputs():
        import jax
        import jax.numpy as jnp
        _gk = jax.random.key(seed)
        x = -0.0002928 + 1 * jax.random.normal(jax.random.fold_in(_gk, 1), (2048, 256), jnp.float32)
        _a = jax.random.bernoulli(jax.random.fold_in(_gk, 2), 0.00195312, (2048, 2048))
        _a = jnp.logical_or(_a, jnp.eye(2048, dtype=bool))
        _af = _a.astype(jnp.float32)
        _af = _af * jax.random.uniform(jax.random.fold_in(_gk, 3), (2048, 2048), jnp.float32, 0.05, 1)
        adj = _af
        return (x, adj)
    x, adj = _rec_inputs()

    def _L0_gnn_setup():
        import jax, jax.numpy as jnp
        import numpy as np
        N, IN_DIM, OUT_DIM = (4096, 256, 256)
        ALPHA = 0.2
        EPS = 1e-09
        key = jax.random.key(seed)
        k1, k2, k3, k4, k5 = jax.random.split(key, 5)
        feat = jax.random.normal(k1, (N, IN_DIM), dtype=jnp.float32)
        counting_attn = jax.random.uniform(k2, (N, N), dtype=jnp.float32)
        W = jax.random.normal(k3, (IN_DIM, OUT_DIM), dtype=jnp.float32) / np.sqrt(IN_DIM)
        attn_l = jax.random.normal(k4, (OUT_DIM, 1), dtype=jnp.float32) * 0.1
        attn_r = jax.random.normal(k5, (OUT_DIM, 1), dtype=jnp.float32) * 0.1
        return {'feat': feat, 'counting_attn': counting_attn, 'W': W, 'attn_l': attn_l, 'attn_r': attn_r}
    _L0_gnn_all = _L0_gnn_setup()
    _L0_gnn_in = {k: v for k, v in _L0_gnn_all.items() if k in ('W', 'attn_l', 'attn_r')}
    del _L0_gnn_all

    def _L0_ffn_setup():
        import jax, jax.numpy as jnp
        import numpy as np
        B, T, D = (4, 512, 256)
        E, TOP_K, H = (8, 2, 128)
        key = jax.random.key(seed)
        ks = jax.random.split(key, 8)
        s = 0.02
        return {'x': jax.random.normal(ks[0], (B, T, D), dtype=jnp.float32), 'router': jax.random.normal(ks[1], (D, E), dtype=jnp.float32) * s, 'shared_gate': jax.random.normal(ks[2], (D, H), dtype=jnp.float32) * s, 'shared_up': jax.random.normal(ks[3], (D, H), dtype=jnp.float32) * s, 'shared_down': jax.random.normal(ks[4], (H, D), dtype=jnp.float32) * s, 'W_gate': jax.random.normal(ks[5], (E, D, H), dtype=jnp.float32) * s, 'W_up': jax.random.normal(ks[6], (E, D, H), dtype=jnp.float32) * s, 'W_down': jax.random.normal(ks[7], (E, H, D), dtype=jnp.float32) * s}
    _L0_ffn_all = _L0_ffn_setup()
    _L0_ffn_in = {k: v for k, v in _L0_ffn_all.items() if k in ('router', 'shared_gate', 'shared_up', 'shared_down', 'W_gate', 'W_up', 'W_down')}
    del _L0_ffn_all

    def _L1_gnn_setup():
        import jax, jax.numpy as jnp
        import numpy as np
        EPS = 1e-08
        key = jax.random.key(seed)
        k1, k2, k3, k4 = jax.random.split(key, 4)
        N, IN, OUT = (4096, 256, 256)
        x = jax.random.normal(k1, (N, IN), dtype=jnp.float32)
        adj = jax.random.uniform(k2, (N, N), dtype=jnp.float32)
        W = jax.random.normal(k3, (OUT, IN), dtype=jnp.float32) * (1.0 / np.sqrt(IN))
        b = jax.random.normal(k4, (OUT,), dtype=jnp.float32) * 0.01
        return {'x': x, 'adj': adj, 'W': W, 'b': b}
    _L1_gnn_all = _L1_gnn_setup()
    _L1_gnn_in = {k: v for k, v in _L1_gnn_all.items() if k in ('W', 'b')}
    del _L1_gnn_all

    def _L1_ffn_setup():
        import jax, jax.numpy as jnp
        import numpy as np
        DIM = 256
        HID = 512
        E = 8
        K = 2
        B, S = (4, 1024)
        key = jax.random.key(seed)
        ks = jax.random.split(key, 10)
        sd = DIM ** (-0.5)
        sh = HID ** (-0.5)
        return {'x': jax.random.normal(ks[0], (B, S, DIM), dtype=jnp.float32), 'gate_w': jax.random.normal(ks[1], (E, DIM), dtype=jnp.float32) * sd, 'biases': jnp.zeros((E,), dtype=jnp.float32), 'w1': jax.random.normal(ks[2], (E, DIM, HID), dtype=jnp.float32) * sd, 'w3': jax.random.normal(ks[3], (E, DIM, HID), dtype=jnp.float32) * sd, 'w2': jax.random.normal(ks[4], (E, HID, DIM), dtype=jnp.float32) * sh, 'sw1': jax.random.normal(ks[5], (DIM, HID), dtype=jnp.float32) * sd, 'sw3': jax.random.normal(ks[6], (DIM, HID), dtype=jnp.float32) * sd, 'sw2': jax.random.normal(ks[7], (HID, DIM), dtype=jnp.float32) * sh}
    _L1_ffn_all = _L1_ffn_setup()
    _L1_ffn_in = {k: v for k, v in _L1_ffn_all.items() if k in ('gate_w', 'biases', 'w1', 'w3', 'w2', 'sw1', 'sw3', 'sw2')}
    del _L1_ffn_all
    return {'x': x, 'adj': adj, 'L0_gnn_W': _L0_gnn_in['W'], 'L0_gnn_attn_l': _L0_gnn_in['attn_l'], 'L0_gnn_attn_r': _L0_gnn_in['attn_r'], 'L0_ffn_router': _L0_ffn_in['router'], 'L0_ffn_shared_gate': _L0_ffn_in['shared_gate'], 'L0_ffn_shared_up': _L0_ffn_in['shared_up'], 'L0_ffn_shared_down': _L0_ffn_in['shared_down'], 'L0_ffn_W_gate': _L0_ffn_in['W_gate'], 'L0_ffn_W_up': _L0_ffn_in['W_up'], 'L0_ffn_W_down': _L0_ffn_in['W_down'], 'L1_gnn_W': _L1_gnn_in['W'], 'L1_gnn_b': _L1_gnn_in['b'], 'L1_ffn_gate_w': _L1_ffn_in['gate_w'], 'L1_ffn_biases': _L1_ffn_in['biases'], 'L1_ffn_w1': _L1_ffn_in['w1'], 'L1_ffn_w3': _L1_ffn_in['w3'], 'L1_ffn_w2': _L1_ffn_in['w2'], 'L1_ffn_sw1': _L1_ffn_in['sw1'], 'L1_ffn_sw3': _L1_ffn_in['sw3'], 'L1_ffn_sw2': _L1_ffn_in['sw2']}

def reference(x, adj, L0_gnn_W, L0_gnn_attn_l, L0_gnn_attn_r, L0_ffn_router, L0_ffn_shared_gate, L0_ffn_shared_up, L0_ffn_shared_down, L0_ffn_W_gate, L0_ffn_W_up, L0_ffn_W_down, L1_gnn_W, L1_gnn_b, L1_ffn_gate_w, L1_ffn_biases, L1_ffn_w1, L1_ffn_w3, L1_ffn_w2, L1_ffn_sw1, L1_ffn_sw3, L1_ffn_sw2):
    import jax
    import jax.numpy as jnp

    def _L0_gnn_ref(feat, counting_attn, W, attn_l, attn_r):
        import jax, jax.numpy as jnp
        import numpy as np
        N, IN_DIM, OUT_DIM = (4096, 256, 256)
        ALPHA = 0.2
        EPS = 1e-09
        h = feat @ W
        a1 = h @ attn_l
        a2 = h @ attn_r
        a = jax.nn.leaky_relu(a1 + a2.T, ALPHA)
        a = a - jnp.max(a, axis=1, keepdims=True)
        nomi = jnp.exp(a) * counting_attn
        deno = jnp.sum(nomi, axis=1, keepdims=True)
        a_nor = nomi / (deno + EPS)
        ret = jax.nn.elu(a_nor @ h)
        return ret

    def _L0_ffn_ref(x, router, shared_gate, shared_up, shared_down, W_gate, W_up, W_down):
        import jax, jax.numpy as jnp
        import numpy as np
        B, T, D = (4, 512, 256)
        E, TOP_K, H = (8, 2, 128)
        b, t, d = x.shape
        n = b * t
        x_flat = x.reshape(n, d)
        shared_out = jax.nn.silu(x_flat @ shared_gate) * (x_flat @ shared_up) @ shared_down
        probs = jax.nn.softmax(x_flat @ router, axis=-1)
        topk_scores, topk_idx = jax.lax.top_k(probs, TOP_K)
        combine = jnp.zeros((n, E), dtype=x.dtype)
        combine = combine.at[jnp.arange(n)[:, None], topk_idx].set(topk_scores)
        gate = jax.nn.silu(jnp.einsum('nd,edh->enh', x_flat, W_gate))
        up = jnp.einsum('nd,edh->enh', x_flat, W_up)
        y = jnp.einsum('enh,ehd->end', gate * up, W_down)
        routed_out = jnp.einsum('ne,end->nd', combine, y)
        return (shared_out + routed_out).reshape(b, t, d)

    def _L1_gnn_ref(x, adj, W, b):
        import jax, jax.numpy as jnp
        import numpy as np
        EPS = 1e-08
        deg = adj.sum(axis=1)
        dis = (deg + EPS) ** (-0.5)
        a_norm = dis[:, None] * adj * dis[None, :]
        h = a_norm @ x
        return h @ W.T + b

    def _L1_ffn_ref(x, gate_w, biases, w1, w3, w2, sw1, sw3, sw2):
        import jax, jax.numpy as jnp
        import numpy as np
        DIM = 256
        HID = 512
        E = 8
        K = 2
        B, S = (4, 1024)
        Bb, Ss, D = x.shape
        xt = x.reshape(Bb * Ss, D)
        shared = jax.nn.silu(xt @ sw1) * (xt @ sw3) @ sw2
        scores = xt @ gate_w.T
        _, idx = jax.lax.top_k(scores + biases, K)
        topv, _ = jax.lax.top_k(scores, K)
        p = jax.nn.sigmoid(topv)
        p = p / jnp.sum(p, axis=-1, keepdims=True)
        h = jax.nn.silu(jnp.einsum('td,edh->eth', xt, w1)) * jnp.einsum('td,edh->eth', xt, w3)
        y = jnp.einsum('eth,ehd->etd', h, w2)
        onehot = jax.nn.one_hot(idx, E, dtype=xt.dtype)
        comb = jnp.einsum('tk,tke->te', p, onehot)
        out = jnp.einsum('te,etd->td', comb, y) + shared
        return out.reshape(Bb, Ss, D)
    x = x + _L0_gnn_ref(_layernorm(x, axis=-1), adj, L0_gnn_W, L0_gnn_attn_l, L0_gnn_attn_r)
    x = x + _L0_ffn_ref(_layernorm(x, axis=-1)[None], L0_ffn_router, L0_ffn_shared_gate, L0_ffn_shared_up, L0_ffn_shared_down, L0_ffn_W_gate, L0_ffn_W_up, L0_ffn_W_down)[0]
    x = x + _L1_gnn_ref(_layernorm(x, axis=-1), adj, L1_gnn_W, L1_gnn_b)
    x = x + _L1_ffn_ref(_layernorm(x, axis=-1)[None], L1_ffn_gate_w, L1_ffn_biases, L1_ffn_w1, L1_ffn_w3, L1_ffn_w2, L1_ffn_sw1, L1_ffn_sw3, L1_ffn_sw2)[0]
    return x

_drawn_inputs = setup_inputs


def setup_inputs(seed=0):
    import zlib

    import numpy as np

    out = dict(_drawn_inputs(seed))
    spreads = {'L1_ffn_biases': (0.0, 0.1)}
    factors = {'L0_ffn_router': 5.252,
     'L0_ffn_W_gate': 4.579,
     'L0_ffn_W_up': 5.071,
     'L0_ffn_W_down': 4.563,
     'L1_gnn_b': 3.072,
     'L0_ffn_shared_gate': 3.073,
     'L0_ffn_shared_up': 2.736,
     'L0_ffn_shared_down': 2.893}
    for name, (base, spread) in spreads.items():
        noise = np.random.default_rng([zlib.crc32(name.encode()), seed]).standard_normal(out[name].shape)
        drawn = base * np.exp(spread * noise) if base else spread * noise
        out[name] = jnp.asarray(drawn.astype(out[name].dtype))
    for name, factor in factors.items():
        out[name] = (out[name] * factor).astype(out[name].dtype)
    return out
```

```python
from contextlib import ExitStack

import concourse.bass as bass
from concourse import mybir

F32 = mybir.dt.float32
F32R = mybir.dt.float32r
I32 = mybir.dt.int32
ACT = mybir.ActivationFunctionType
ALU = mybir.AluOpType
AX = mybir.AxisListType.X
PE = mybir.EngineType.PE

P = 128
N = 2048
D = 256
T = N // P
C = D // P
E = 8
TOP_K = 2
H0 = 128
H1 = 512
HC1 = H1 // P
HALF = N // 2
GW = D + 2
LN_EPS = 1e-5
ATT_EPS = 1e-9
DEG_EPS = 1e-8
EXP_CLAMP = 75.0
ROUTED_TILES = (N * TOP_K + E * (P - 1)) // P
SHARED_TILES = T
FFN1_TILES = SHARED_TILES + ROUTED_TILES
SLOT_ROWS = ROUTED_TILES * P
BIG = 3.0e38


def wait_from(eng, semaphore, value):
    if isinstance(value, int) and value <= 0:
        return
    eng.wait_ge(semaphore, value)


class Chain:

    def __init__(self, eng, semaphore):
        self.eng, self.semaphore, self.count = eng, semaphore, 0

    def __call__(self, instruction):
        self.count += 1
        instruction.then_inc(self.semaphore, 1)
        self.eng.wait_ge(self.semaphore, self.count)


class Pool:

    def __init__(self, nc, ctx, prefix):
        self.nc, self.ctx, self.prefix = nc, ctx, prefix

    def sb(self, name, shape, dtype=F32):
        return self.ctx.enter_context(self.nc.sbuf_tensor(self.prefix + name, shape, dtype))

    def ps(self, name, shape):
        return self.ctx.enter_context(self.nc.psum_tensor(self.prefix + name, shape, F32))

    def sem(self, name):
        return self.ctx.enter_context(self.nc.semaphore(self.prefix + name))


class Norm:

    def __init__(self, pool, Y=None):
        self.stats = pool.sb("ln_stats", [P, T * 6])
        self.mv = pool.sb("ln_mean_var", [P, T, 2])
        self.std = pool.sb("ln_std", [P, T])
        self.rstd = pool.sb("ln_rstd", [P, T])
        self.Y = pool.sb("Y", [P, T * D]) if Y is None else Y
        self.YTh = pool.sb("YTh", [P, C, N], F32R)
        self.YTl = pool.sb("YTl", [P, C, N], F32R)
        self.psT = [pool.ps(f"psT{i}", [P, 512]) for i in range(2)]
        self.stats_done = pool.sem("ln_stats_done")
        self.mv_done = pool.sem("ln_mean_var_done")
        self.std_done = pool.sem("ln_std_done")
        self.rstd_done = pool.sem("ln_rstd_done")
        self.normed = pool.sem("ln_normed")
        self.transposed = pool.sem("y_transposed")
        self.hi_done = pool.sem("yt_hi_done")
        self.lo_done = pool.sem("yt_lo_done")


def norm_vector(nc, dve, X, n, x_loaded=None):
    for g in range(4):
        if x_loaded is not None:
            dve.wait_ge(x_loaded[g], 16)
        with dve.Fori(4 * g, 4 * g + 4) as t:
            nc.vector.bn_stats(n.stats[:, bass.ts(t, 6)], X[:, bass.ts(t, D)]).then_inc(n.stats_done, 1)
    dve.wait_ge(n.stats_done, T)
    for t in range(T):
        nc.vector.bn_aggr(n.mv[:, t, :], n.stats[:, 6 * t:6 * t + 6]).then_inc(n.mv_done, 1)
    dve.wait_ge(n.std_done, 1)
    nc.vector.reciprocal(n.rstd[:], n.std[:]).then_inc(n.rstd_done, 1)
    dve.wait_ge(n.rstd_done, 1)
    for t in range(T):
        nc.vector.tensor_scalar(n.Y[:, t * D:(t + 1) * D], X[:, t * D:(t + 1) * D], n.mv[:, t, 0:1],
                                n.rstd[:, t:t + 1], ALU.subtract, ALU.mult).then_inc(n.normed, 1)


def norm_vector_lo(nc, dve, n, g):
    dve.wait_ge(n.hi_done, g + 1)
    cols = slice(2 * P * g, 2 * P * (g + 1))
    nc.vector.tensor_tensor(n.YTl[:, :, cols], n.psT[g % 2][:].rearrange("p (c n) -> p c n", c=C),
                            n.YTh[:, :, cols].bitcast(F32), ALU.subtract).then_inc(n.lo_done, 1)


def norm_scalar_std(nc, act, top, n):
    act.wait_ge(n.mv_done, T)
    nc.scalar.activation(n.std[:], n.mv[:, :, 1], ACT.Sqrt, bias=top.eps[:, 0:1]).then_inc(n.std_done, 1)


def norm_scalar_hi(nc, act, n):
    for g in range(T // 2):
        act.wait_ge(n.transposed, g + 1)
        cols = slice(2 * P * g, 2 * P * (g + 1))
        nc.scalar.activation(n.YTh[:, :, cols], n.psT[g % 2][:].rearrange("p (c n) -> p c n", c=C),
                             ACT.Copy).then_inc(n.hi_done, 1)


def norm_tensor(nc, pe, n, ident):
    for g in range(T // 2):
        pe.wait_ge(n.normed, 2 * g + 2)
        wait_from(pe, n.lo_done, g - 1)
        for c in range(C):
            for s in range(2):
                t = 2 * g + s
                last = nc.tensor.transpose(n.psT[g % 2][:, (2 * c + s) * P:(2 * c + s + 1) * P],
                                           n.Y[:, t * D + c * P:t * D + (c + 1) * P], ident[:])
        last.then_inc(n.transposed, 1)


def matmul3(nc, out, lhs, rhs, start, stop, skip=False):
    nc.tensor.matmul(out, lhs[0], rhs[0], start=start, stop=False, skip_group_check=skip)
    nc.tensor.matmul(out, lhs[0], rhs[1], start=False, stop=False, skip_group_check=skip)
    return nc.tensor.matmul(out, lhs[1], rhs[0], start=False, stop=stop, skip_group_check=skip)


def attention_features(nc, dram, top, att):
    with ExitStack() as ctx:
        pool = Pool(nc, ctx, "f_")
        n = Norm(pool)
        Wf = pool.sb("W", [P, C, GW])
        Wh = pool.sb("Wh", [P, C, GW], F32R)
        Wl = pool.sb("Wl", [P, C, GW], F32R)
        WT = pool.sb("WT", [P, C, D])
        attn = pool.sb("attn", [P, C, 2])
        WB = pool.sb("WB", [P, 2, C, P])
        WBh = pool.sb("WBh", [P, 2, C, P], F32R)
        WBl = pool.sb("WBl", [P, 2, C, P], F32R)
        Hs = pool.sb("Hs", [P, T, GW])
        max4 = pool.sb("max4", [P, 4])
        amax = pool.sb("amax", [P, 1])
        dmax = pool.sb("dmax", [P, T])
        srow = pool.sb("srow", [P, T])
        V = pool.sb("V", [P, T])
        zeros = pool.sb("zeros", [P, D])
        psA = pool.ps("psA", [P, 512])
        psR = [pool.ps(f"psR{i}", [P, 512]) for i in range(4)]

        x_loaded = [pool.sem(f"x_loaded{g}") for g in range(4)]
        w_loaded = pool.sem("w_loaded")
        zeroed = pool.sem("zeroed")
        wlr_done = pool.sem("wlr_done")
        wf_done = pool.sem("wf_done")
        w_hi = pool.sem("w_hi")
        w_lo = pool.sem("w_lo")
        bc_done = pool.sem("bc_done")
        max_done = pool.sem("max_done")
        s_done = pool.sem("s_done")
        h_done = pool.sem("h_done")
        hs_done = pool.sem("hs_done")
        chain = pool.sem("chain")
        exp_in = pool.sem("exp_in")
        exp_done = pool.sem("exp_done")
        ones_done = pool.sem("ones_done")
        g_hi = pool.sem("g_hi")
        g_lo = pool.sem("g_lo")
        filled = pool.sem("filled")

        with nc.Block() as block:
            @block.sync
            def _(sp):
                xv = dram["x"].rearrange("(t p) d -> p t d", p=P)
                Xv = top.X[:].rearrange("p (t d) -> p t d", t=T)
                for g in range(4):
                    sp.dma_start(Xv[:, 4 * g:4 * g + 4, :], xv[:, 4 * g:4 * g + 4, :]).then_inc(x_loaded[g], 16)
                sp.dma_start(top.ident[:], dram["ident"]).then_inc(w_loaded, 16)
                sp.dma_start(WT[:], dram["L0_gnn_WT"].rearrange("(c p) d -> p c d", p=P)).then_inc(w_loaded, 16)
                sp.dma_start(Wf[:, :, 0:D], dram["L0_gnn_W"].rearrange("(c p) d -> p c d", p=P)).then_inc(w_loaded, 16)
                sp.dma_start(attn[:], dram["attn"].rearrange("(c p) a -> p c a", p=P)).then_inc(w_loaded, 16)
                sp.dma_start(top.table[:], dram["table"]).then_inc(w_loaded, 16)
                sp.wait_ge(zeroed, 1)
                sp.dma_start(dram["slots_in"][SHARED_TILES * P:, :].rearrange("(a p) d -> p a d", p=P),
                             zeros[:].unsqueeze(1).to_broadcast([P, ROUTED_TILES, D])).then_inc(filled, 16)
                sp.wait_ge(filled, 16)

            @block.vector
            def _(dve):
                nc.vector.memset(zeros[:], 0.0).then_inc(zeroed, 1)
                nc.vector.memset(top.eps[:, 0:1], LN_EPS).then_inc(top.eps_set, 1)
                nc.vector.memset(top.eps[:, 1:2], DEG_EPS).then_inc(top.eps_set, 1)
                norm_vector(nc, dve, top.X, n, x_loaded)
                dve.wait_ge(wlr_done, 1)
                nc.vector.tensor_copy(Wf[:, :, D:GW], psA[:, 0:2 * C].rearrange("p (c a) -> p c a", c=C)).then_inc(wf_done, 1)
                dve.wait_ge(wf_done, 1)
                for c in range(C):
                    for a in range(2):
                        nc.vector.tensor_copy(WB[:, a, c, :], Wf[:, c, D + a:D + a + 1].to_broadcast([P, P])).then_inc(wf_done, 1)
                dve.wait_ge(w_hi, 2)
                nc.vector.tensor_tensor(Wl[:], Wf[:], Wh[:].bitcast(F32), ALU.subtract).then_inc(w_lo, 1)
                nc.vector.tensor_tensor(WBl[:], WB[:], WBh[:].bitcast(F32), ALU.subtract).then_inc(w_lo, 1)
                for g in range(T // 2):
                    norm_vector_lo(nc, dve, n, g)
                for q in range(4):
                    dve.wait_ge(bc_done, q + 1)
                    nc.vector.reduce_max(max4[:, q:q + 1], psR[q][:], AX).then_inc(max_done, 1)
                dve.wait_ge(max_done, 4)
                step = Chain(dve, chain)
                step(nc.vector.reduce_max(amax[:], max4[:], AX))
                for q in range(4):
                    dve.wait_ge(bc_done, 4 + q + 1)
                    nc.vector.tensor_scalar(att.R[:, 512 * q:512 * q + 512], psR[q][:], amax[:], EXP_CLAMP,
                                            ALU.add, ALU.min).then_inc(s_done, 1)
                dve.wait_ge(hs_done, T)
                nc.vector.tensor_scalar(dmax[:], Hs[:, :, D + 1], amax[:], None, ALU.subtract).then_inc(exp_in, 1)
                step(nc.vector.tensor_scalar(srow[:], Hs[:, :, D], amax[:], EXP_CLAMP, ALU.add, ALU.min))
                nc.vector.tensor_scalar(att.S[:], srow[:], 0.0, None, ALU.max).then_inc(exp_in, 1)
                dve.wait_ge(exp_in, 2)
                nc.vector.memset(Hs[:, :, D:GW], 1.0).then_inc(ones_done, 1)
                for t in range(T):
                    dve.wait_ge(g_hi, t + 1)
                    nc.vector.scalar_tensor_tensor(att.Gl[:, t * GW:(t + 1) * GW], Hs[:, t, :], V[:, t:t + 1],
                                                   att.Gh[:, t * GW:(t + 1) * GW].bitcast(F32),
                                                   ALU.mult, ALU.subtract).then_inc(g_lo, 1)

            @block.scalar
            def _(act):
                act.wait_ge(top.eps_set, 2)
                norm_scalar_std(nc, act, top, n)
                act.wait_ge(wf_done, 1 + 2 * C)
                nc.scalar.activation(Wh[:], Wf[:], ACT.Copy).then_inc(w_hi, 1)
                nc.scalar.activation(WBh[:], WB[:], ACT.Copy).then_inc(w_hi, 1)
                norm_scalar_hi(nc, act, n)
                for t in range(T):
                    act.wait_ge(h_done, t + 1)
                    nc.scalar.activation(Hs[:, t, :], n.psT[t % 2][:, 0:GW], ACT.Copy).then_inc(hs_done, 1)
                for q in range(4):
                    act.wait_ge(s_done, q + 1)
                    nc.scalar.activation(att.R[:, 512 * q:512 * q + 512], att.R[:, 512 * q:512 * q + 512],
                                         ACT.Exp, scale=0.8).then_inc(exp_done, 1)
                act.wait_ge(exp_in, 2)
                nc.scalar.activation(V[:], dmax[:], ACT.Exp, scale=0.2).then_inc(exp_done, 1)
                nc.scalar.activation(att.EA[:], dmax[:], ACT.Exp, scale=0.8).then_inc(exp_done, 1)
                nc.scalar.activation(att.EQ[:], att.S[:], ACT.Exp, scale=-0.8).then_inc(exp_done, 1)
                act.wait_ge(exp_done, 7)
                act.wait_ge(ones_done, 1)
                for t in range(T):
                    nc.scalar.activation(att.Gh[:, t * GW:(t + 1) * GW], Hs[:, t, :], ACT.Copy,
                                         scale=V[:, t:t + 1]).then_inc(g_hi, 1)

            @block.tensor
            def _(pe):
                pe.wait_ge(w_loaded, 5 * 16)
                for c in range(C):
                    for k in range(C):
                        last = nc.tensor.matmul(psA[:, 2 * c:2 * c + 2], WT[:, k, c * P:(c + 1) * P], attn[:, k, :],
                                                start=(k == 0), stop=(k == C - 1))
                last.then_inc(wlr_done, 1)
                norm_tensor(nc, pe, n, top.ident)
                pe.wait_ge(w_lo, 2)
                pe.wait_ge(n.lo_done, T // 2)
                for a in (1, 0):
                    for q in range(4):
                        if a == 0:
                            pe.wait_ge(max_done, q + 1)
                        cols = slice(512 * q, 512 * q + 512)
                        for c in range(C):
                            last = matmul3(nc, psR[q][:], (WBh[:, a, c, :], WBl[:, a, c, :]),
                                           (n.YTh[:, c, cols], n.YTl[:, c, cols]), c == 0, c == C - 1)
                        last.then_inc(bc_done, 1)
                for t in range(T):
                    wait_from(pe, hs_done, t - 1)
                    tok = slice(t * P, (t + 1) * P)
                    for c in range(C):
                        last = matmul3(nc, n.psT[t % 2][:, 0:GW], (n.YTh[:, c, tok], n.YTl[:, c, tok]),
                                       (Wh[:, c, :], Wl[:, c, :]), c == 0, c == C - 1)
                    last.then_inc(h_done, 1)


def attention_sums(nc, dram, top, att):
    BUFS = 4
    HT = HALF // P
    with ExitStack() as ctx:
        pool = Pool(nc, ctx, "s_")
        adj = [pool.sb(f"adj{b}", [P, HALF]) for b in range(BUFS)]
        expo = [pool.sb(f"expo{b}", [P, HALF]) for b in range(2)]
        w = [pool.sb(f"w{b}", [P, HALF]) for b in range(2)]
        wh = [pool.sb(f"wh{b}", [P, HALF], F32R) for b in range(2)]
        wl = [pool.sb(f"wl{b}", [P, HALF], F32R) for b in range(2)]
        O = [pool.sb(f"O{h}", [P, HT, GW]) for h in range(2)]
        neg = [pool.sb(f"neg{h}", [P, HT, D]) for h in range(2)]
        den = pool.sb("den", [P, T])
        sums = [pool.ps(f"sums{i}", [P, 512]) for i in range(HT)]
        adj_loaded = [pool.sem(f"adj_loaded{b}") for b in range(BUFS)]
        expo_done = pool.sem("expo_done")
        w_done = pool.sem("w_done")
        hi_done = pool.sem("hi_done")
        lo_done = pool.sem("lo_done")
        mm_done = pool.sem("mm_done")
        bank_done = pool.sem("bank_done")
        evac_done = pool.sem("evac_done")
        chain = pool.sem("chain")
        neg_done = pool.sem("neg_done")
        elu_exp = pool.sem("elu_exp")
        adjT = dram["adjT"]

        with nc.Block() as block:
            @block.sync
            def _(sp):
                def load(half, j4):
                    for b in range(BUFS):
                        j = j4 * BUFS + b
                        wait_from(sp, w_done, half * T + j - (BUFS - 1))
                        sp.dma_start(adj[b][:], adjT[bass.ds(j * P, P), half * HALF:(half + 1) * HALF])\
                          .then_inc(adj_loaded[b], 16)
                load(0, 0)
                with sp.Fori(1, T // BUFS) as j4:
                    load(0, j4)
                with sp.Fori(0, T // BUFS) as j4:
                    load(1, j4)

            @block.scalar
            def _(act):
                def expo_step(half, j, b):
                    wait_from(act, w_done, half * T + j - 1)
                    nc.scalar.activation(expo[b][:], att.R[:, half * HALF:(half + 1) * HALF], ACT.Relu, bias=-1.0,
                                         scale=att.EA[:, bass.ds(j, 1)]).then_inc(expo_done, 1)

                def hi_step(half, j, b):
                    act.wait_ge(w_done, half * T + j + 1)
                    wait_from(act, mm_done, half * T + j - 1)
                    nc.scalar.activation(wh[b][:], w[b][:], ACT.Copy).then_inc(hi_done, 1)

                expo_step(0, 0, 0)
                for half in range(2):
                    def pair(j2, last=False):
                        expo_step(half, 2 * j2 + 1, 1)
                        hi_step(half, 2 * j2, 0)
                        if not last:
                            expo_step(half, 2 * j2 + 2, 0)
                        elif half == 0:
                            expo_step(1, 0, 0)
                        hi_step(half, 2 * j2 + 1, 1)
                    pair(0)
                    with act.Fori(1, T // 2 - 1) as j2:
                        pair(j2)
                    pair(T // 2 - 1, last=True)
                    for i in range(HT):
                        if i < HT - 1:
                            act.wait_ge(bank_done, half * (HT - 1) + i + 1)
                        else:
                            act.wait_ge(mm_done, (half + 1) * T)
                        nc.scalar.activation(O[half][:, i, :], sums[i][:, 0:GW], ACT.Copy).then_inc(evac_done, 1)
                for half in range(2):
                    act.wait_ge(neg_done, half + 1)
                    nc.scalar.activation(neg[half][:], neg[half][:], ACT.Exp).then_inc(elu_exp, 1)

            @block.vector
            def _(dve):
                def w_step(half, j, jq, b4, b2):
                    dve.wait_ge(adj_loaded[b4], 16 * (half * (T // BUFS) + jq + 1))
                    dve.wait_ge(expo_done, half * T + j + 1)
                    wait_from(dve, lo_done, half * T + j - 1)
                    nc.vector.scalar_tensor_tensor(w[b2][:], expo[b2][:], 1.0, adj[b4][:], ALU.add, ALU.mult)\
                      .then_inc(w_done, 1)

                def lo_step(u, b2):
                    dve.wait_ge(hi_done, u + 1)
                    wait_from(dve, mm_done, u - 1)
                    nc.vector.tensor_tensor(wl[b2][:], w[b2][:], wh[b2][:].bitcast(F32), ALU.subtract)\
                      .then_inc(lo_done, 1)

                for half in range(2):
                    def four(jq, first=False):
                        for s in range(4):
                            j = jq * 4 + s
                            w_step(half, j, jq, s, s % 2)
                            if not (first and s == 0 and half == 0):
                                lo_step(half * T + j - 1, (s + 1) % 2)
                    four(0, first=True)
                    with dve.Fori(1, T // 4) as jq:
                        four(jq)
                lo_step(2 * T - 1, 1)
                step = Chain(dve, chain)
                for half in range(2):
                    dve.wait_ge(evac_done, (half + 1) * HT)
                    eq = att.EQ[:, half * HT:(half + 1) * HT]
                    dn = den[:, half * HT:(half + 1) * HT]
                    step(nc.vector.tensor_tensor(dn, O[half][:, :, D], eq, ALU.mult))
                    step(nc.vector.tensor_scalar(dn, dn, ATT_EPS, None, ALU.add))
                    step(nc.vector.reciprocal(dn, dn))
                    step(nc.vector.tensor_tensor(dn, dn, eq, ALU.mult))
                    step(nc.vector.tensor_tensor(O[half][:, :, 0:D], O[half][:, :, 0:D],
                                                 dn.unsqueeze(2).to_broadcast([P, HT, D]), ALU.mult))
                    nc.vector.tensor_scalar(neg[half][:], O[half][:, :, 0:D], 0.0, None, ALU.min).then_inc(neg_done, 1)
                for half in range(2):
                    xs = top.X[:, half * HT * D:(half + 1) * HT * D].rearrange("p (t d) -> p t d", t=HT)
                    dve.wait_ge(elu_exp, half + 1)
                    step(nc.vector.scalar_tensor_tensor(O[half][:, :, 0:D], O[half][:, :, 0:D], 0.0, neg[half][:],
                                                        ALU.max, ALU.add))
                    step(nc.vector.scalar_tensor_tensor(xs, O[half][:, :, 0:D], -1.0, xs, ALU.add, ALU.add))

            @block.tensor
            def _(pe):
                def unit(half, j, b, start=False, stop=False):
                    pe.wait_ge(lo_done, half * T + j + 1)
                    g = (att.Gh[:, bass.ts(j, GW)], att.Gl[:, bass.ts(j, GW)])
                    for i in range(HT):
                        if start and half == 1:
                            pe.wait_ge(evac_done, i + 1)
                        tok = slice(i * P, (i + 1) * P)
                        last = matmul3(nc, sums[i][:, 0:GW], (wh[b][:, tok], wl[b][:, tok]), g, start, stop)
                        if stop and i < HT - 1:
                            last.then_inc(bank_done, 1)
                    last.then_inc(mm_done, 1)
                for half in range(2):
                    unit(half, 0, 0, start=True)
                    unit(half, 1, 1)
                    with pe.Fori(1, T // 2 - 1) as j2:
                        unit(half, 2 * j2, 0)
                        unit(half, 2 * j2 + 1, 1)
                    unit(half, T - 2, 0)
                    unit(half, T - 1, 1, stop=True)


class Gate:
    def __init__(self, pool):
        self.eq = pool.sb("g_eq", [P, T, E])
        self.rank = pool.sb("g_rank", [P, T, E])
        self.rest = pool.sb("g_rest", [P, T, E])
        self.best = pool.sb("g_best", [P, T])


def over_experts(col):
    return col.unsqueeze(2).to_broadcast([P, T, E])


def over_tiles(row):
    return row.unsqueeze(1).to_broadcast([P, T, row.shape[-1]])


def top_two(nc, step, g, wt, src, m1, m2, first, second):
    for m, hot, s in ((m1, first, src), (m2, second, g.rest)):
        step(nc.vector.reduce_max(m[:], s[:], AX))
        step(nc.vector.tensor_tensor(g.eq[:], s[:], over_experts(m[:]), ALU.is_equal))
        step(nc.vector.tensor_tensor(g.rank[:], g.eq[:], over_tiles(wt), ALU.mult))
        step(nc.vector.reduce_max(g.best[:], g.rank[:], AX))
        step(nc.vector.tensor_tensor(hot[:], g.rank[:], over_experts(g.best[:]), ALU.is_equal))
        if hot is first:
            step(nc.vector.scalar_tensor_tensor(g.rest[:].rearrange("p t e -> p (t e)"),
                                                first[:].rearrange("p t e -> p (t e)"), -BIG,
                                                src[:].rearrange("p t e -> p (t e)"), ALU.mult, ALU.add))


def router_tensor(nc, pe, n, bank, router, done):
    for t in range(T):
        tok = slice(t * P, (t + 1) * P)
        for c in range(C):
            last = matmul3(nc, bank[:, t * E:(t + 1) * E], (n.YTh[:, c, tok], n.YTl[:, c, tok]),
                           (router[0][:, c, :], router[1][:, c, :]), c == 0, c == C - 1)
    last.then_inc(done, 1)


def mixture_dense(nc, dram, top):
    U = 5
    UW = [2, 2, 2, 2, 1]
    EW = 2 * H0
    NE = E + 1
    with ExitStack() as ctx:
        pool = Pool(nc, ctx, "m_")
        n = Norm(pool)
        g = Gate(pool)
        GUf = pool.sb("GUf", [P, C, NE * EW])
        Df = pool.sb("Df", [P, NE * D])
        rf = pool.sb("rf", [P, C, E])
        GU = [pool.sb("GUh", [P, C, NE * EW], F32R), pool.sb("GUl", [P, C, NE * EW], F32R)]
        Dn = [pool.sb("Dnh", [P, NE * D], F32R), pool.sb("Dnl", [P, NE * D], F32R)]
        router = [pool.sb("rh", [P, C, E], F32R), pool.sb("rl", [P, C, E], F32R)]
        xT = [pool.sb(f"xT{b}", [P, 2, C, P], F32R) for b in range(2)]
        adjn = [pool.sb(f"adjn{b}", [P, N]) for b in range(2)]
        sg = [pool.sb(f"sg{b}", [P, 2, H0]) for b in range(2)]
        h = [pool.sb(f"h{b}", [P, 2 * H0]) for b in range(2)]
        hTh = [pool.sb(f"hTh{b}", [P, 2 * P], F32R) for b in range(2)]
        hTl = [pool.sb(f"hTl{b}", [P, 2 * P], F32R) for b in range(2)]
        logits = pool.sb("logits", [P, T, E])
        prob = pool.sb("prob", [P, T, E])
        hot1 = pool.sb("hot1", [P, T, E])
        hot2 = pool.sb("hot2", [P, T, E])
        comb = pool.sb("comb", [P, T * NE])
        m1 = pool.sb("m1", [P, T])
        m2 = pool.sb("m2", [P, T])
        psGU = [pool.ps(f"psGU{b}", [P, 512]) for b in range(2)]
        psHT = [pool.ps(f"psHT{b}", [P, 512]) for b in range(2)]
        psY = [pool.ps(f"psY{b}", [P, 512]) for b in range(2)]

        weights_loaded = pool.sem("weights_loaded")
        adjn_loaded = [pool.sem(f"adjn_loaded{b}") for b in range(2)]
        xt_loaded = [pool.sem(f"xt_loaded{b}") for b in range(2)]
        w_hi = pool.sem("w_hi")
        w_lo = pool.sem("w_lo")
        logits_done = pool.sem("logits_done")
        chain = pool.sem("chain")
        shifted = pool.sem("shifted")
        exped = pool.sem("exped")
        gu_done = pool.sem("gu_done")
        silu_done = pool.sem("silu_done")
        h_done = pool.sem("h_done")
        ht_done = pool.sem("ht_done")
        hi_done = pool.sem("hi_done")
        lo_done = pool.sem("lo_done")
        down_done = pool.sem("down_done")
        y_done = pool.sem("y_done")
        deg_done = pool.sem("deg_done")

        with nc.Block() as block:
            @block.sync
            def _(sp):
                sp.dma_start(GUf[:], dram["L0_gu"].rearrange("(c p) n -> p c n", p=P)).then_inc(weights_loaded, 16)
                sp.dma_start(Df[:], dram["L0_down"]).then_inc(weights_loaded, 16)
                sp.dma_start(rf[:], dram["L0_ffn_router"].rearrange("(c p) e -> p c e", p=P)).then_inc(weights_loaded, 16)
                sp.wait_ge(n.lo_done, T // 2)

                def tile(i, b):
                    t = 2 * i + b
                    wait_from(sp, gu_done, U * (t - 1))
                    for part, YT in enumerate((n.YTh, n.YTl)):
                        sp.dma_start(xT[b][:, part, :, :].bitcast(F32), YT[:, :, bass.ts(t, P)].bitcast(F32)).then_inc(xt_loaded[b], 16)
                    wait_from(sp, deg_done, t - 1)
                    sp.dma_start(adjn[b][:], dram["adj"][bass.ts(t, P), :]).then_inc(adjn_loaded[b], 16)
                tile(0, 0)
                tile(0, 1)
                with sp.Fori(1, T // 2) as i:
                    tile(i, 0)
                    tile(i, 1)

            @block.scalar
            def _(act):
                norm_scalar_std(nc, act, top, n)
                act.wait_ge(weights_loaded, 48)
                nc.scalar.activation(router[0][:], rf[:], ACT.Copy).then_inc(w_hi, 1)
                nc.scalar.activation(GU[0][:], GUf[:], ACT.Copy).then_inc(w_hi, 1)
                nc.scalar.activation(Dn[0][:], Df[:], ACT.Copy).then_inc(w_hi, 1)
                norm_scalar_hi(nc, act, n)
                act.wait_ge(shifted, 1)
                nc.scalar.activation(prob[:], prob[:], ACT.Exp).then_inc(exped, 1)

                def silu(k, q, b):
                    act.wait_ge(gu_done, k + 1)
                    wait_from(act, h_done, k - 1)
                    v = psGU[b][:, 0:UW[q] * EW].rearrange("p (e k h) -> p e k h", e=UW[q], k=2)
                    nc.scalar.activation(sg[b][:, 0:UW[q], :], v[:, :, 0, :], ACT.Silu).then_inc(silu_done, 1)

                def hi(k, q, b):
                    act.wait_ge(ht_done, k + 1)
                    wait_from(act, down_done, k - 1)
                    nc.scalar.activation(hTh[b][:, 0:UW[q] * P], psHT[b][:, 0:UW[q] * P], ACT.Copy)\
                      .then_inc(hi_done, 1)

                def pair(i, first=False):
                    for v in range(2 * U):
                        k = 2 * U * i + v
                        silu(k, v % U, v % 2)
                        if not (first and v == 0):
                            hi(k - 1, (v - 1) % U, (v - 1) % 2)
                        if v % U == 3:
                            act.wait_ge(adjn_loaded[v // U], 16 * (i + 1))
                            nc.scalar.activation(adjn[v // U][:], adjn[v // U][:], ACT.Copy,
                                                 accum_out=top.deg[:, bass.ds(2 * i + v // U, 1)]).then_inc(deg_done, 1)
                pair(0, first=True)
                with act.Fori(1, T // 2) as i:
                    pair(i)
                hi(T * U - 1, U - 1, 1)

            @block.vector
            def _(dve):
                norm_vector(nc, dve, top.X, n)
                dve.wait_ge(w_hi, 3)
                nc.vector.tensor_tensor(router[1][:], rf[:], router[0][:].bitcast(F32), ALU.subtract).then_inc(w_lo, 1)
                nc.vector.tensor_tensor(GU[1][:], GUf[:], GU[0][:].bitcast(F32), ALU.subtract).then_inc(w_lo, 1)
                nc.vector.tensor_tensor(Dn[1][:], Df[:], Dn[0][:].bitcast(F32), ALU.subtract).then_inc(w_lo, 1)
                for q in range(T // 2):
                    norm_vector_lo(nc, dve, n, q)
                step = Chain(dve, chain)
                dve.wait_ge(logits_done, 1)
                step(nc.vector.tensor_copy(logits[:], psY[0][:, 0:T * E].rearrange("p (t e) -> p t e", t=T)))
                step(nc.vector.reduce_max(m1[:], logits[:], AX))
                nc.vector.tensor_tensor(prob[:], logits[:], over_experts(m1[:]), ALU.subtract).then_inc(shifted, 1)
                dve.wait_ge(exped, 1)
                step(nc.vector.reduce_sum(m1[:], prob[:], AX))
                step(nc.vector.reciprocal(m2[:], m1[:]))
                step(nc.vector.tensor_tensor(prob[:], prob[:], over_experts(m2[:]), ALU.mult))
                top_two(nc, step, g, top.consts["wt"], prob, m1, m2, hot1, hot2)
                step(nc.vector.tensor_tensor(hot1[:], hot1[:], hot2[:], ALU.add))
                cv = comb[:].rearrange("p (t e) -> p t e", t=T)
                step(nc.vector.memset(cv[:, :, E:NE], 1.0))
                step(nc.vector.tensor_tensor(cv[:, :, 0:E], prob[:], hot1[:], ALU.mult))

                def make_h(k, t, q, b):
                    dve.wait_ge(silu_done, k + 1)
                    wait_from(dve, ht_done, k - 1)
                    for s in range(UW[q]):
                        last = nc.vector.scalar_tensor_tensor(
                            h[b][:, s * H0:(s + 1) * H0], sg[b][:, s, :], comb[:, bass.ds(NE * t + 2 * q + s, 1)],
                            psGU[b][:, s * EW + H0:(s + 1) * EW], ALU.mult, ALU.mult)
                    last.then_inc(h_done, 1)

                def lo(k, q, b):
                    dve.wait_ge(hi_done, k + 1)
                    wait_from(dve, down_done, k - 1)
                    nc.vector.tensor_tensor(hTl[b][:, 0:UW[q] * P], psHT[b][:, 0:UW[q] * P],
                                            hTh[b][:, 0:UW[q] * P].bitcast(F32), ALU.subtract).then_inc(lo_done, 1)

                def add_y(t, b):
                    dve.wait_ge(down_done, U * (t + 1))
                    xs = top.X[:, bass.ts(t, D)]
                    nc.vector.tensor_tensor(xs, xs, psY[b][:, 0:D], ALU.add).then_inc(y_done, 1)

                def pair(i, first=False):
                    for v in range(2 * U):
                        k, s = 2 * U * i + v, v // U
                        make_h(k, 2 * i + s, v % U, v % 2)
                        if not (first and v == 0):
                            lo(k - 1, (v - 1) % U, (v - 1) % 2)
                        if v % U == 2 and not (first and s == 0):
                            add_y(2 * i + s - 1, (s + 1) % 2)
                pair(0, first=True)
                with dve.Fori(1, T // 2) as i:
                    pair(i)
                lo(T * U - 1, U - 1, 1)
                add_y(T - 1, 1)
                dve.wait_ge(y_done, T)

            @block.tensor
            def _(pe):
                norm_tensor(nc, pe, n, top.ident)
                pe.wait_ge(w_lo, 3)
                pe.wait_ge(n.lo_done, T // 2)
                router_tensor(nc, pe, n, psY[0], router, logits_done)

                def gate_up(i, k, q, s, b):
                    if q == 0:
                        pe.wait_ge(xt_loaded[s], 32 * (i + 1))
                    wait_from(pe, h_done, k - 1)
                    cols = slice(2 * q * EW, (2 * q + UW[q]) * EW)
                    for c in range(C):
                        last = matmul3(nc, psGU[b][:, 0:UW[q] * EW], (xT[s][:, 0, c, :], xT[s][:, 1, c, :]),
                                       (GU[0][:, c, cols], GU[1][:, c, cols]), c == 0, c == C - 1)
                    last.then_inc(gu_done, 1)

                def transpose_h(k, q, b):
                    pe.wait_ge(h_done, k + 1)
                    wait_from(pe, lo_done, k - 1)
                    for s in range(UW[q]):
                        last = nc.tensor.transpose(psHT[b][:, s * P:(s + 1) * P], h[b][:, s * H0:(s + 1) * H0],
                                                   top.ident[:])
                    last.then_inc(ht_done, 1)

                def down(k, t, q, s, b):
                    pe.wait_ge(lo_done, k + 1)
                    if q == 0:
                        wait_from(pe, y_done, t - 1)
                        if isinstance(t, int) and t == 0:
                            pe.wait_ge(chain, 1)
                    for x in range(UW[q]):
                        e = 2 * q + x
                        last = matmul3(nc, psY[s][:, 0:D], (hTh[b][:, x * P:(x + 1) * P], hTl[b][:, x * P:(x + 1) * P]),
                                       (Dn[0][:, e * D:(e + 1) * D], Dn[1][:, e * D:(e + 1) * D]), e == 0, e == NE - 1)
                    last.then_inc(down_done, 1)

                def pair(i, first=False):
                    for v in range(2 * U):
                        k, s = 2 * U * i + v, v // U
                        gate_up(i, k, v % U, s, v % 2)
                        if not (first and v < 1):
                            transpose_h(k - 1, (v - 1) % U, (v - 1) % 2)
                        if not (first and v < 2):
                            sd = ((v - 2) % (2 * U)) // U
                            td = 2 * i + s if v % U >= 2 else 2 * i + s - 1
                            down(k - 2, td, (v - 2) % U, sd, v % 2)
                pair(0, first=True)
                with pe.Fori(1, T // 2) as i:
                    pair(i)
                last_k = T * U - 1
                transpose_h(last_k, U - 1, 1)
                down(last_k - 1, T - 1, U - 2, 1, 0)
                down(last_k, T - 1, U - 1, 1, 1)


def convolution(nc, dram, top):
    BUFS = 3
    with ExitStack() as ctx:
        pool = Pool(nc, ctx, "c_")
        Z = [pool.sb("Zh", [P, T * D], F32R), pool.sb("Zl", [P, T * D], F32R)]
        dis = pool.sb("dis", [P, T])
        sq = pool.sb("sq", [P, T])
        bias = pool.sb("bias", [P, D])
        deg_sqrt = pool.sem("deg_sqrt")
        dis_done = pool.sem("dis_done")
        loads = pool.sem("loads")
        with ExitStack() as inner:
            part = Pool(nc, inner, "ca_")
            n = Norm(part)
            Wf = part.sb("W", [P, C, D])
            W = [part.sb("Wh", [P, C, D], F32R), part.sb("Wl", [P, C, D], F32R)]
            psZ = [part.ps(f"psZ{b}", [P, 512]) for b in range(4)]
            w_hi = part.sem("w_hi")
            w_lo = part.sem("w_lo")
            z_done = part.sem("z_done")
            z_hi = part.sem("z_hi")
            z_lo = part.sem("z_lo")
            bias_added = part.sem("bias_added")
            with nc.Block() as block:
                @block.sync
                def _(sp):
                    sp.dma_start(Wf[:], dram["L1_gnn_WT"].rearrange("(c p) n -> p c n", p=P)).then_inc(loads, 16)
                    sp.dma_start(bias[:], dram["bias_rows"]).then_inc(loads, 16)

                @block.scalar
                def _(act):
                    nc.scalar.activation(sq[:], top.deg[:], ACT.Sqrt, bias=top.eps[:, 1:2]).then_inc(deg_sqrt, 1)
                    norm_scalar_std(nc, act, top, n)
                    act.wait_ge(loads, 32)
                    nc.scalar.activation(W[0][:], Wf[:], ACT.Copy).then_inc(w_hi, 1)
                    norm_scalar_hi(nc, act, n)
                    act.wait_ge(dis_done, 1)
                    for t in range(T):
                        act.wait_ge(z_done, t + 1)
                        nc.scalar.activation(Z[0][:, t * D:(t + 1) * D], psZ[t % 4][:, 0:D], ACT.Copy,
                                             scale=dis[:, t:t + 1]).then_inc(z_hi, 1)

                @block.vector
                def _(dve):
                    norm_vector(nc, dve, top.X, n)
                    dve.wait_ge(deg_sqrt, 1)
                    nc.vector.reciprocal(dis[:], sq[:]).then_inc(dis_done, 1)
                    dve.wait_ge(w_hi, 1)
                    nc.vector.tensor_tensor(W[1][:], Wf[:], W[0][:].bitcast(F32), ALU.subtract).then_inc(w_lo, 1)
                    for q in range(T // 2):
                        norm_vector_lo(nc, dve, n, q)
                    dve.wait_ge(loads, 32)
                    Xv = top.X[:].rearrange("p (t d) -> p t d", t=T)
                    dve.wait_ge(n.normed, T)
                    nc.vector.tensor_tensor(Xv, Xv, bias[:].unsqueeze(1).to_broadcast([P, T, D]), ALU.add)\
                      .then_inc(bias_added, 1)
                    dve.wait_ge(dis_done, 1)
                    for t in range(T):
                        dve.wait_ge(z_hi, t + 1)
                        nc.vector.scalar_tensor_tensor(Z[1][:, t * D:(t + 1) * D], psZ[t % 4][:, 0:D], dis[:, t:t + 1],
                                                       Z[0][:, t * D:(t + 1) * D].bitcast(F32),
                                                       ALU.mult, ALU.subtract).then_inc(z_lo, 1)

                @block.tensor
                def _(pe):
                    norm_tensor(nc, pe, n, top.ident)
                    pe.wait_ge(w_lo, 1)
                    pe.wait_ge(n.lo_done, T // 2)
                    for t in range(T):
                        wait_from(pe, z_lo, t - 3)
                        tok = slice(t * P, (t + 1) * P)
                        for c in range(C):
                            last = matmul3(nc, psZ[t % 4][:, 0:D], (n.YTh[:, c, tok], n.YTl[:, c, tok]),
                                           (W[0][:, c, :], W[1][:, c, :]), c == 0, c == C - 1)
                        last.then_inc(z_done, 1)

        with ExitStack() as inner:
            part = Pool(nc, inner, "cb_")
            adj = [part.sb(f"adj{b}", [P, N]) for b in range(BUFS)]
            ah = [part.sb(f"ah{b}", [P, N], F32R) for b in range(2)]
            al = [part.sb(f"al{b}", [P, N], F32R) for b in range(2)]
            sums = [part.ps(f"sums{i}", [P, 512]) for i in range(T // 2)]
            adj_loaded = [part.sem(f"adj_loaded{b}") for b in range(BUFS)]
            hi_done = part.sem("hi_done")
            lo_done = part.sem("lo_done")
            mm_done = part.sem("mm_done")
            bank_done = part.sem("bank_done")
            x_done = part.sem("x_done")
            with nc.Block() as block:
                @block.sync
                def _(sp):
                    for j in range(T):
                        wait_from(sp, lo_done, j - BUFS + 1)
                        sp.dma_start(adj[j % BUFS][:], dram["adjT"][j * P:(j + 1) * P, :])\
                          .then_inc(adj_loaded[j % BUFS], 16)

                @block.scalar
                def _(act):
                    for j in range(T):
                        act.wait_ge(adj_loaded[j % BUFS], 16 * (j // BUFS + 1))
                        wait_from(act, mm_done, j - 1)
                        nc.scalar.activation(ah[j % 2][:], adj[j % BUFS][:], ACT.Copy).then_inc(hi_done, 1)

                @block.vector
                def _(dve):
                    for j in range(T):
                        dve.wait_ge(hi_done, j + 1)
                        wait_from(dve, mm_done, j - 1)
                        nc.vector.tensor_tensor(al[j % 2][:], adj[j % BUFS][:], ah[j % 2][:].bitcast(F32),
                                                ALU.subtract).then_inc(lo_done, 1)
                    for i in range(T):
                        if i // 2 < T // 2 - 1:
                            dve.wait_ge(bank_done, i // 2 + 1)
                        else:
                            dve.wait_ge(mm_done, T)
                        xs = top.X[:, i * D:(i + 1) * D]
                        nc.vector.scalar_tensor_tensor(xs, sums[i // 2][:, (i % 2) * D:(i % 2 + 1) * D],
                                                       dis[:, i:i + 1], xs, ALU.mult, ALU.add).then_inc(x_done, 1)
                    dve.wait_ge(x_done, T)

                @block.tensor
                def _(pe):
                    def unit(j, b, start=False, stop=False):
                        pe.wait_ge(lo_done, j + 1)
                        z = (Z[0][:, bass.ts(j, D)], Z[1][:, bass.ts(j, D)])
                        for i in range(T):
                            tok = slice(i * P, (i + 1) * P)
                            last = matmul3(nc, sums[i // 2][:, (i % 2) * D:(i % 2 + 1) * D],
                                           (ah[b][:, tok], al[b][:, tok]), z, start and i % 2 == 0, stop, skip=True)
                            if stop and i % 2 == 1 and i < T - 1:
                                last.then_inc(bank_done, 1)
                        last.then_inc(mm_done, 1)
                    unit(0, 0, start=True)
                    unit(1, 1)
                    with pe.Fori(1, T // 2 - 1) as j2:
                        unit(2 * j2, 0)
                        unit(2 * j2 + 1, 1)
                    unit(T - 2, 0)
                    unit(T - 1, 1, stop=True)


def mixture_routed(nc, dram, top):
    NE = E + 1
    G1 = C * H1
    D1 = HC1 * D
    with ExitStack() as ctx:
        pool = Pool(nc, ctx, "r_")
        Y = pool.sb("Y", [P, T * D])
        Wg = pool.sb("Wg", [P, NE * G1])
        Wu = pool.sb("Wu", [P, NE * G1])
        Wd = pool.sb("Wd", [P, NE * D1])
        pos = [pool.sb(f"pos{k}", [P, T], I32) for k in range(2)]
        p = [pool.sb(f"p{k}", [P, T]) for k in range(2)]
        emap = pool.sb("emap", [1, FFN1_TILES], I32)
        shared_loaded = pool.sem("shared_loaded")
        routed_loaded = pool.sem("routed_loaded")

        with ExitStack() as inner:
            part = Pool(nc, inner, "ra_")
            n = Norm(part, Y)
            g = Gate(part)
            rf = part.sb("rf", [P, C, E])
            router = [part.sb("rh", [P, C, E], F32R), part.sb("rl", [P, C, E], F32R)]
            eb = part.sb("expert_bias", [P, E])
            scores = part.sb("scores", [P, T, E])
            biased = part.sb("biased", [P, T, E])
            hot = [part.sb(f"hot{k}", [P, T, E]) for k in range(2)]
            spare = [part.sb(f"spare{k}", [P, T, E]) for k in range(2)]
            both = part.sb("both", [P, T * E])
            v = [part.sb(f"v{k}", [P, T]) for k in range(2)]
            u = [part.sb(f"u{k}", [P, T]) for k in range(2)]
            totB = part.sb("totB", [P, P])
            cmp16 = part.sb("cmp16", [P, E, T])
            ntile = part.sb("ntile", [P, E])
            cumm = part.sb("cumm", [P, E, E])
            cum = part.sb("cum", [P, E])
            base = part.sb("base", [P, E])
            slot = part.sb("slot", [P, T, E])
            picked = part.sb("picked", [P, T, E])
            posf = part.sb("posf", [P, T])
            cmpt = part.sb("cmpt", [1, ROUTED_TILES, E])
            emapf = part.sb("emapf", [1, FFN1_TILES])
            psL = part.ps("psL", [P, 512])
            psS = part.ps("psS", [P, 512])
            psC = part.ps("psC", [P, 512])
            psTot = part.ps("psTot", [P, 512])
            small_loaded = part.sem("small_loaded")
            w_hi = part.sem("w_hi")
            w_lo = part.sem("w_lo")
            logits_done = part.sem("logits_done")
            both_done = part.sem("both_done")
            tot_done = part.sem("tot_done")
            totb_done = part.sem("totb_done")
            count_done = part.sem("count_done")
            chain = part.sem("chain")
            sig_in = part.sem("sig_in")
            sig_done = part.sem("sig_done")
            ct = top.consts
            with nc.Block() as block:
                @block.sync
                def _(sp):
                    sp.dma_start(rf[:], dram["L1_router"].rearrange("(c p) e -> p c e", p=P)).then_inc(small_loaded, 16)
                    sp.dma_start(eb[:], dram["expert_bias_rows"]).then_inc(small_loaded, 16)
                    for e in (E, *range(E)):
                        done = shared_loaded if e == E else routed_loaded
                        sp.dma_start(Wg[:, e * G1:(e + 1) * G1].rearrange("p (c n) -> p c n", c=C),
                                     dram["L1_gate"][e].rearrange("(c p) n -> p c n", p=P)).then_inc(done, 16)
                        sp.dma_start(Wu[:, e * G1:(e + 1) * G1].rearrange("p (c n) -> p c n", c=C),
                                     dram["L1_up"][e].rearrange("(c p) n -> p c n", p=P)).then_inc(done, 16)
                        sp.dma_start(Wd[:, e * D1:(e + 1) * D1].rearrange("p (c n) -> p c n", c=HC1),
                                     dram["L1_down"][e].rearrange("(c p) n -> p c n", p=P)).then_inc(done, 16)

                @block.scalar
                def _(act):
                    norm_scalar_std(nc, act, top, n)
                    act.wait_ge(small_loaded, 32)
                    nc.scalar.activation(router[0][:], rf[:], ACT.Copy).then_inc(w_hi, 1)
                    norm_scalar_hi(nc, act, n)
                    act.wait_ge(sig_in, 1)
                    for k in range(2):
                        nc.scalar.activation(u[k][:], v[k][:], ACT.Sigmoid).then_inc(sig_done, 1)

                @block.vector
                def _(dve):
                    norm_vector(nc, dve, top.X, n)
                    dve.wait_ge(w_hi, 1)
                    nc.vector.tensor_tensor(router[1][:], rf[:], router[0][:].bitcast(F32), ALU.subtract).then_inc(w_lo, 1)
                    for q in range(T // 2):
                        norm_vector_lo(nc, dve, n, q)
                    step = Chain(dve, chain)
                    dve.wait_ge(logits_done, 1)
                    step(nc.vector.tensor_copy(scores[:], psL[:, 0:T * E].rearrange("p (t e) -> p t e", t=T)))
                    step(nc.vector.tensor_tensor(biased[:], scores[:], over_tiles(eb[:]), ALU.add))
                    top_two(nc, step, g, ct["wt"], biased, v[0], v[1], hot[0], hot[1])
                    nc.vector.tensor_tensor(both[:].rearrange("p (t e) -> p t e", t=T), hot[0][:], hot[1][:], ALU.add)\
                      .then_inc(both_done, 1)
                    top_two(nc, step, g, ct["wt"], scores, v[0], v[1], spare[0], spare[1])
                    nc.vector.memset(emapf[:], float(E)).then_inc(sig_in, 1)
                    dve.wait_ge(sig_done, 2)
                    step(nc.vector.tensor_tensor(v[0][:], u[0][:], u[1][:], ALU.add))
                    step(nc.vector.reciprocal(v[1][:], v[0][:]))
                    for k in range(2):
                        step(nc.vector.tensor_tensor(p[k][:], u[k][:], v[1][:], ALU.mult))
                    dve.wait_ge(tot_done, 1)
                    nc.vector.tensor_copy(totB[:], psTot[:, 0:1].to_broadcast([P, P])).then_inc(totb_done, 1)
                    dve.wait_ge(count_done, 1)
                    step(nc.vector.tensor_tensor(cmp16[:], psC[:, 0:E].unsqueeze(2).to_broadcast([P, E, T]),
                                                 ct["multiples"].unsqueeze(1).to_broadcast([P, E, T]), ALU.is_gt))
                    step(nc.vector.reduce_sum(ntile[:], cmp16[:], AX))
                    step(nc.vector.tensor_tensor(cumm[:], ct["upto"].rearrange("p (a b) -> p a b", a=E),
                                                 ntile[:].unsqueeze(1).to_broadcast([P, E, E]), ALU.mult))
                    step(nc.vector.reduce_sum(cum[:], cumm[:], AX))
                    step(nc.vector.tensor_tensor(base[:], cum[:], ntile[:], ALU.subtract))
                    step(nc.vector.tensor_scalar(base[:], base[:], float(P), float(SHARED_TILES * P), ALU.mult, ALU.add))
                    step(nc.vector.tensor_tensor(slot[:], psS[:, 0:T * E].rearrange("p (t e) -> p t e", t=T),
                                                 over_tiles(base[:]), ALU.add))
                    for k in range(2):
                        step(nc.vector.tensor_tensor(picked[:], slot[:], hot[k][:], ALU.mult))
                        step(nc.vector.reduce_sum(posf[:], picked[:], AX))
                        step(nc.vector.tensor_copy(pos[k][:], posf[:]))
                    step(nc.vector.tensor_tensor(cmpt[:], ct["tile_index"].rearrange("p (a b) -> p a b", a=ROUTED_TILES),
                                                 cum[0:1, :].unsqueeze(1).to_broadcast([1, ROUTED_TILES, E]), ALU.is_ge))
                    step(nc.vector.reduce_sum(emapf[:, SHARED_TILES:], cmpt[:], AX))
                    step(nc.vector.tensor_scalar(emapf[:, SHARED_TILES:], emapf[:, SHARED_TILES:], float(E - 1), None, ALU.min))
                    step(nc.vector.tensor_copy(emap[:], emapf[:]))

                @block.tensor
                def _(pe):
                    norm_tensor(nc, pe, n, top.ident)
                    pe.wait_ge(w_lo, 1)
                    pe.wait_ge(n.lo_done, T // 2)
                    router_tensor(nc, pe, n, psL, router, logits_done)
                    pe.wait_ge(both_done, 1)
                    nc.tensor.matmul(psTot[:, 0:1], both[:], ct["ones"], start=True, stop=True).then_inc(tot_done, 1)
                    pe.wait_ge(totb_done, 1)
                    nc.tensor.matmul(psS[:, 0:T * E], totB[:], ct["earlier_tile"], start=True, stop=False)
                    nc.tensor.matmul(psS[:, 0:T * E], ct["before"], both[:], start=False, stop=True)
                    nc.tensor.matmul(psC[:, 0:E], totB[:], ct["same_expert"], start=True, stop=True).then_inc(count_done, 1)

        with ExitStack() as inner:
            part = Pool(nc, inner, "rb_")
            xrow = [part.sb(f"xrow{b}", [P, D]) for b in range(2)]
            xT = [part.sb(f"xT{b}", [P, D]) for b in range(2)]
            sg = [part.sb(f"sg{b}", [P, H1]) for b in range(2)]
            h = [part.sb(f"h{b}", [P, H1]) for b in range(2)]
            hT = [part.sb(f"hT{b}", [P, H1]) for b in range(2)]
            yo = [part.sb(f"yo{b}", [P, D]) for b in range(2)]
            Y2 = part.sb("Y2", [P, T * D])
            psG = [part.ps(f"psG{b}", [P, 512]) for b in range(2)]
            psU = [part.ps(f"psU{b}", [P, 512]) for b in range(2)]
            psT = part.ps("psT", [P, 512])
            psHT = part.ps("psHT", [P, 512])
            psY = [part.ps(f"psY{b}", [P, 512]) for b in range(2)]
            ln_stored = part.sem("ln_stored")
            scattered = part.sem("scattered")
            xrow_loaded = [part.sem(f"xrow_loaded{b}") for b in range(2)]
            y_stored = [part.sem(f"y_stored{b}") for b in range(2)]
            t_done = part.sem("t_done")
            xt_done = part.sem("xt_done")
            gate_done = part.sem("gate_done")
            up_done = part.sem("up_done")
            silu_done = part.sem("silu_done")
            h_done = part.sem("h_done")
            ht_done = part.sem("ht_done")
            htc_done = part.sem("htc_done")
            down_done = part.sem("down_done")
            y_done = part.sem("y_done")
            shared_back = part.sem("shared_back")
            got = [part.sem(f"got{t}") for t in range(T)]
            chain = part.sem("chain")
            final = part.sem("final")
            stored = part.sem("stored")
            M = FFN1_TILES
            rows_in, rows_out = dram["slots_in"], dram["slots_out"]
            Yv = Y[:].rearrange("p (t d) -> p t d", t=T)
            Y2v = Y2[:].rearrange("p (t d) -> p t d", t=T)
            with nc.Block() as block:
                @block.sync
                def _(sp):
                    sp.dma_start(rows_in[0:N, :].rearrange("(t p) d -> p t d", p=P), Yv).then_inc(ln_stored, 16)
                    sp.wait_ge(ln_stored, 16)

                    def tile(m, b, i):
                        wait_from(sp, t_done, m - 1)
                        sp.dma_start(xrow[b][:], rows_in[bass.ts(m, P), :]).then_inc(xrow_loaded[b], 16)
                        if not isinstance(m, int) or m >= 4:
                            store(m - 4, b)

                    def store(m, b):
                        sp.wait_ge(y_done, m + 1)
                        sp.dma_start(rows_out[bass.ts(m, P), :], yo[b][:]).then_inc(y_stored[b], 16)
                    for m in range(4):
                        tile(m, m % 2, None)
                    with sp.Fori(2, SHARED_TILES // 2) as i:
                        tile(2 * i, 0, i)
                        tile(2 * i + 1, 1, i)
                    sp.wait_ge(scattered, 16 * TOP_K * T)
                    with sp.Fori(SHARED_TILES // 2, M // 2) as i:
                        tile(2 * i, 0, i)
                        tile(2 * i + 1, 1, i)
                    tile(M - 1, 0, None)
                    for m in range(M - 4, M):
                        store(m, m % 2)
                    sp.wait_ge(y_stored[0], 16 * ((M + 1) // 2))
                    sp.wait_ge(y_stored[1], 16 * (M // 2))
                    sp.dma_start(Y2v, rows_out[0:N, :].rearrange("(t p) d -> p t d", p=P)).then_inc(shared_back, 16)
                    for q in range(4):
                        sp.wait_ge(final, 4 * (q + 1))
                        sp.dma_start(dram["out"].rearrange("(t p) d -> p t d", p=P)[:, 4 * q:4 * q + 4, :],
                                     top.X[:].rearrange("p (t d) -> p t d", t=T)[:, 4 * q:4 * q + 4, :]).then_inc(stored, 16)
                    sp.wait_ge(stored, 64)

                @block.gpsimd
                def _(pool_eng):
                    for t in range(T):
                        for k in range(TOP_K):
                            nc.gpsimd.indirect_dma_start(rows_in, bass.IndirectOffsetOnAxis(ap=pos[k][:, t:t + 1], axis=0),
                                                         Y[:, t * D:(t + 1) * D], None).then_inc(scattered, 16)
                    pool_eng.wait_ge(ln_stored, 16)
                    pool_eng.wait_ge(scattered, 16 * TOP_K * T)
                    pool_eng.wait_ge(y_stored[0], 16 * ((M + 1) // 2))
                    pool_eng.wait_ge(y_stored[1], 16 * (M // 2))
                    for t in range(T):
                        nc.gpsimd.indirect_dma_start(Y[:, t * D:(t + 1) * D], None, rows_out,
                                                     bass.IndirectOffsetOnAxis(ap=pos[0][:, t:t + 1], axis=0)).then_inc(got[t], 16)
                    pool_eng.wait_ge(chain, T)
                    for t in range(T):
                        nc.gpsimd.indirect_dma_start(Y2[:, t * D:(t + 1) * D], None, rows_out,
                                                     bass.IndirectOffsetOnAxis(ap=pos[1][:, t:t + 1], axis=0)).then_inc(got[t], 16)

                @block.scalar
                def _(act):
                    def silu(m, b):
                        act.wait_ge(gate_done, m + 1)
                        wait_from(act, h_done, m - 1)
                        nc.scalar.activation(sg[b][:], psG[b][:], ACT.Silu).then_inc(silu_done, 1)

                    def copy_ht(m, b):
                        act.wait_ge(ht_done, m + 1)
                        wait_from(act, down_done, m - 1)
                        nc.scalar.activation(hT[b][:], psHT[:], ACT.Copy).then_inc(htc_done, 1)
                    silu(0, 0)

                    def pair(i):
                        silu(2 * i + 1, 1)
                        copy_ht(2 * i, 0)
                        silu(2 * i + 2, 0)
                        copy_ht(2 * i + 1, 1)
                    pair(0)
                    with act.Fori(1, M // 2) as i:
                        pair(i)
                    copy_ht(M - 1, 0)

                @block.vector
                def _(dve):
                    def copy_xt(m, b):
                        dve.wait_ge(t_done, m + 1)
                        wait_from(dve, up_done, m - 1)
                        nc.vector.tensor_copy(xT[b][:], psT[:, 0:D]).then_inc(xt_done, 1)

                    def make_h(m, b):
                        dve.wait_ge(silu_done, m + 1)
                        dve.wait_ge(up_done, m + 1)
                        wait_from(dve, ht_done, m - 1)
                        nc.vector.tensor_tensor(h[b][:], sg[b][:], psU[b][:], ALU.mult).then_inc(h_done, 1)

                    def copy_y(m, b, i):
                        dve.wait_ge(down_done, m + 1)
                        if not isinstance(m, int) or m >= 2:
                            dve.wait_ge(y_stored[b], 16 * i)
                        nc.vector.tensor_copy(yo[b][:], psY[b][:, 0:D]).then_inc(y_done, 1)

                    def unit(m, b, i=None):
                        make_h(m, b)
                        if not (isinstance(m, int) and m == M - 1):
                            copy_xt(m + 1, 1 - b)
                        if not (isinstance(m, int) and m == 0):
                            copy_y(m - 1, 1 - b, i)
                    copy_xt(0, 0)
                    unit(0, 0)
                    unit(1, 1, 0)
                    unit(2, 0, 0)
                    with dve.Fori(1, M // 2 - 1) as i:
                        unit(2 * i + 1, 1, i)
                        unit(2 * i + 2, 0, i)
                    unit(M - 2, 1, M // 2 - 1)
                    unit(M - 1, 0, M // 2 - 1)
                    copy_y(M - 1, 0, M // 2)
                    dve.wait_ge(shared_back, 16)
                    for t in range(T):
                        xs = slice(t * D, (t + 1) * D)
                        nc.vector.tensor_tensor(top.X[:, xs], top.X[:, xs], Y2[:, xs], ALU.add).then_inc(chain, 1)
                    dve.wait_ge(chain, T)
                    for t in range(T):
                        xs = slice(t * D, (t + 1) * D)
                        dve.wait_ge(got[t], 32)
                        nc.vector.scalar_tensor_tensor(top.X[:, xs], Y[:, xs], p[0][:, t:t + 1], top.X[:, xs],
                                                       ALU.mult, ALU.add).then_inc(chain, 1)
                        dve.wait_ge(chain, T + t + 1)
                        nc.vector.scalar_tensor_tensor(top.X[:, xs], Y2[:, xs], p[1][:, t:t + 1], top.X[:, xs],
                                                       ALU.mult, ALU.add).then_inc(final, 1)

                @block.tensor
                def _(pe):
                    def transpose_x(m, b, i):
                        pe.wait_ge(xrow_loaded[b], 16 * (i + 1))
                        wait_from(pe, xt_done, m)
                        for c in range(C):
                            last = nc.tensor.transpose(psT[:, c * P:(c + 1) * P], xrow[b][:, c * P:(c + 1) * P],
                                                       top.ident[:])
                        last.then_inc(t_done, 1)

                    def gate(m, b, W, bank, e, done):
                        for c in range(C):
                            last = nc.tensor.matmul(bank[:], xT[b][:, c * P:(c + 1) * P], W[:, bass.ds((e * C + c) * H1, H1)],
                                                    start=(c == 0), stop=(c == C - 1))
                        last.then_inc(done, 1)

                    def transpose_h(m, b):
                        pe.wait_ge(h_done, m + 1)
                        wait_from(pe, htc_done, m)
                        for c in range(HC1):
                            last = nc.tensor.transpose(psHT[:, c * P:(c + 1) * P], h[b][:, c * P:(c + 1) * P], top.ident[:])
                        last.then_inc(ht_done, 1)

                    def down(m, b, e):
                        pe.wait_ge(htc_done, m + 1)
                        wait_from(pe, y_done, m - 1)
                        for c in range(HC1):
                            last = nc.tensor.matmul(psY[b][:, 0:D], hT[b][:, c * P:(c + 1) * P],
                                                    Wd[:, bass.ds((e * HC1 + c) * D, D)], start=(c == 0), stop=(c == HC1 - 1))
                        last.then_inc(down_done, 1)

                    def expert(m):
                        if isinstance(m, int) and m < SHARED_TILES:
                            return E
                        return nc.values_load(emap[0:1, bass.ds(m, 1)], engines=[PE], min_val=0, max_val=E,
                                              skip_runtime_bounds_check_because="counted among 8 experts and clamped")

                    def unit(m, b, i_next, last=False):
                        e = expert(m)
                        pe.wait_ge(xt_done, m + 1)
                        wait_from(pe, silu_done, m - 1)
                        gate(m, b, Wg, psG[b], e, gate_done)
                        transpose = not (isinstance(m, int) and m == 0)
                        if transpose:
                            transpose_h(m - 1, 1 - b)
                        gate(m, b, Wu, psU[b], e, up_done)
                        if not last:
                            transpose_x(m + 1, 1 - b, i_next)
                        if transpose:
                            down(m - 1, 1 - b, expert(m - 1))
                    pe.wait_ge(shared_loaded, 48)
                    transpose_x(0, 0, 0)
                    unit(0, 0, 0)
                    unit(1, 1, 1)
                    unit(2, 0, 1)
                    with pe.Fori(1, SHARED_TILES // 2 - 1) as i:
                        unit(2 * i + 1, 1, i + 1)
                        unit(2 * i + 2, 0, i + 1)
                    pe.wait_ge(routed_loaded, 48 * E)
                    with pe.Fori(SHARED_TILES // 2 - 1, M // 2 - 1) as i:
                        unit(2 * i + 1, 1, i + 1)
                        unit(2 * i + 2, 0, i + 1)
                    unit(M - 2, 1, M // 2)
                    unit(M - 1, 0, None, last=True)
                    transpose_h(M - 1, 0)
                    down(M - 1, 0, expert(M - 1))


class Top:
    pass


CONSTS = {"wt": E, "multiples": T, "upto": E * E, "ones": 1, "before": P, "earlier_tile": P, "same_expert": E,
          "tile_index": ROUTED_TILES * E}


def host_constants(np):
    k = np.arange(P)
    e = np.arange(E)
    rows = {
        "wt": np.tile(E - e, (P, 1)),
        "multiples": np.tile(P * np.arange(T), (P, 1)),
        "upto": np.tile((e[None, :] <= e[:, None]).reshape(1, -1), (P, 1)),
        "ones": np.ones((P, 1)),
        "before": k[:, None] < k[None, :],
        "earlier_tile": (k[:, None] % E == k[None, :] % E) & (k[:, None] // E < k[None, :] // E),
        "same_expert": k[:, None] % E == e[None, :],
        "tile_index": np.tile(np.repeat(np.arange(ROUTED_TILES), E), (P, 1)),
    }
    return np.concatenate([rows[name].astype(np.float32) for name in CONSTS], axis=1)


def program(nc, dram):
    dram["slots_in"] = nc.dram_tensor("slots_in", (FFN1_TILES * P, D), F32).ap()
    dram["slots_out"] = nc.dram_tensor("slots_out", (FFN1_TILES * P, D), F32).ap()
    with ExitStack() as ctx:
        pool = Pool(nc, ctx, "")
        top = Top()
        top.X = pool.sb("X", [P, T * D])
        top.ident = pool.sb("ident", [P, P])
        top.deg = pool.sb("deg", [P, T])
        top.eps = pool.sb("eps", [P, 2])
        top.eps_set = pool.sem("eps_set")
        width = sum(CONSTS.values())
        table = pool.sb("table", [P, width])
        top.table = table
        top.consts, at = {}, 0
        for name, wd in CONSTS.items():
            rows = 1 if name == "tile_index" else P
            top.consts[name] = table[0:rows, at:at + wd]
            at += wd
        with ExitStack() as a:
            att_pool = Pool(nc, a, "a_")
            att = Top()
            att.R = att_pool.sb("R", [P, N])
            att.S = att_pool.sb("S", [P, T])
            att.EA = att_pool.sb("EA", [P, T])
            att.EQ = att_pool.sb("EQ", [P, T])
            att.Gh = att_pool.sb("Gh", [P, T * GW], F32R)
            att.Gl = att_pool.sb("Gl", [P, T * GW], F32R)
            attention_features(nc, dram, top, att)
            attention_sums(nc, dram, top, att)
        mixture_dense(nc, dram, top)
        convolution(nc, dram, top)
        mixture_routed(nc, dram, top)


def kernel(**inputs):
    import numpy as np
    import concourse.bacc as bacc
    from concourse.bass_utils import run_bass_kernel_spmd as run

    v = {name: np.asarray(a) for name, a in inputs.items()}
    arrays = {name: v[name] for name in ("x", "adj", "L0_gnn_W", "L0_ffn_router")}
    arrays["attn"] = np.concatenate([v["L0_gnn_attn_l"], v["L0_gnn_attn_r"]], axis=1)
    arrays["ident"] = np.eye(P, dtype=np.float32)
    arrays["table"] = host_constants(np)
    arrays["adjT"] = v["adj"].T
    arrays["L0_gnn_WT"] = v["L0_gnn_W"].T
    gate = np.concatenate([v["L0_ffn_W_gate"], v["L0_ffn_shared_gate"][None]])
    up = np.concatenate([v["L0_ffn_W_up"], v["L0_ffn_shared_up"][None]])
    down = np.concatenate([v["L0_ffn_W_down"], v["L0_ffn_shared_down"][None]])
    arrays["L0_gu"] = np.concatenate([gate, up], axis=2).transpose(1, 0, 2).reshape(D, -1)
    arrays["L0_down"] = down.transpose(1, 0, 2).reshape(H0, -1)
    arrays["L1_gnn_WT"] = v["L1_gnn_W"].T
    arrays["bias_rows"] = np.broadcast_to(v["L1_gnn_b"][None], (P, D))
    arrays["L1_router"] = v["L1_ffn_gate_w"].T
    arrays["expert_bias_rows"] = np.broadcast_to(v["L1_ffn_biases"][None], (P, E))
    arrays["L1_gate"] = np.concatenate([v["L1_ffn_w1"], v["L1_ffn_sw1"][None]])
    arrays["L1_up"] = np.concatenate([v["L1_ffn_w3"], v["L1_ffn_sw3"][None]])
    arrays["L1_down"] = np.concatenate([v["L1_ffn_w2"], v["L1_ffn_sw2"][None]])
    arrays = {"in_" + name: np.ascontiguousarray(a) for name, a in arrays.items()}

    nc = bacc.Bacc("TRN2", target_bir_lowering=False, num_devices=1)
    dram = {name[3:]: nc.dram_tensor(name, a.shape, mybir.dt.from_np(a.dtype), kind="ExternalInput").ap()
            for name, a in arrays.items()}
    dram["out"] = nc.dram_tensor("out", (N, D), F32, kind="ExternalOutput").ap()
    program(nc, dram)
    return run(nc, [arrays], core_ids=[0]).results[0]["out"]
```
